# Optimizing a Trainium2 kernel written in Bass

```python
import numpy as np
import jax
import jax.numpy as jnp

def _softmax(x, axis=-1):
    return jax.nn.softmax(x, axis=axis)

def _gelu(x):
    return jax.nn.gelu(x, approximate=True)

def _silu(x):
    return jax.nn.silu(x)

def _sigmoid(x):
    return jax.nn.sigmoid(x)

def _layernorm(x, axis=-1, eps=1e-05):
    m = jnp.mean(x, axis=axis, keepdims=True)
    v = jnp.var(x, axis=axis, keepdims=True)
    return (x - m) / jnp.sqrt(v + eps)

def _scatter_add(tgt, idx, src, axis=0):
    return tgt.at[idx].add(src)

def _segment_sum(src, seg, n):
    return jax.ops.segment_sum(src, seg, n)
kernel_name = 'mk_adaln_attn_ffn_d1_seqx_r8_e7a19d'

def setup_inputs(seed: int=0):
    np.random.seed(seed)
    _w = jnp.asarray

    def _rec_inputs():
        import jax
        import jax.numpy as jnp
        _rk = jax.random.key(seed)
        x = 8.748e-05 + 1 * jax.random.normal(jax.random.fold_in(_rk, 1), (4, 256, 256), jnp.float32)
        _lenS = 256 - jax.random.randint(jax.random.fold_in(_rk, 7), (4,), 0, max(1, 256 // 4) + 1, jnp.int32)
        _lenS2 = 256 - jax.random.randint(jax.random.fold_in(_rk, 8), (4,), 0, max(1, 256 // 4) + 1, jnp.int32)
        cond_2048 = -9.80646e-05 + 1.00041 * jax.random.normal(jax.random.fold_in(_rk, 11), (4, 256), jnp.float32)
        return (x, cond_2048)
    x, cond_2048 = _rec_inputs()

    def _L0_cond_setup():
        import jax, jax.numpy as jnp
        import numpy as np
        DT = 0.01
        EPSILON = 0.08
        ALPHA = 0.7
        BETA = 0.8
        CLAMP = 20.0
        B, T, N = (32, 128, 256)

        def _derivative(q, p, drive, coupling, bias):
            i_couple = jnp.tanh(q) @ coupling.T
            dq = q - q ** 3 / 3.0 - p + drive + i_couple + bias
            dp = EPSILON * (q + ALPHA - BETA * p)
            return (dq, dp)

        def _rk4_step(q, p, drive, coupling, bias):
            dq1, dp1 = _derivative(q, p, drive, coupling, bias)
            dq2, dp2 = _derivative(q + 0.5 * DT * dq1, p + 0.5 * DT * dp1, drive, coupling, bias)
            dq3, dp3 = _derivative(q + 0.5 * DT * dq2, p + 0.5 * DT * dp2, drive, coupling, bias)
            dq4, dp4 = _derivative(q + DT * dq3, p + DT * dp3, drive, coupling, bias)
            q_next = q + DT / 6.0 * (dq1 + 2 * dq2 + 2 * dq3 + dq4)
            p_next = p + DT / 6.0 * (dp1 + 2 * dp2 + 2 * dp3 + dp4)
            q_next = jnp.clip(q_next, -CLAMP, CLAMP)
            p_next = jnp.clip(p_next, -CLAMP, CLAMP)
            return (q_next, p_next)
        key = jax.random.key(seed)
        k1, k2, k3, k4 = jax.random.split(key, 4)
        return {'q0': jax.random.normal(k1, (B, N), dtype=jnp.float32), 'p0': jax.random.normal(k2, (B, N), dtype=jnp.float32), 'input_drive_seq': jax.random.normal(k3, (B, T, N), dtype=jnp.float32), 'coupling': jax.random.normal(k4, (N, N), dtype=jnp.float32) * 0.01, 'bias': jnp.zeros((N,), dtype=jnp.float32)}
    _L0_cond_all = _L0_cond_setup()
    _L0_cond_in = {k: v for k, v in _L0_cond_all.items() if k in ('coupling', 'bias')}
    del _L0_cond_all

    def _L0_attn_setup():
        import jax, jax.numpy as jnp
        import numpy as np
        B, T, D_MODEL = (4, 256, 256)
        NUM_HEADS, HEAD_SIZE = (16, 128)
        MODEL_SIZE = 256
        key = jax.random.key(seed)
        ks = jax.random.split(key, 9)
        s = 0.02 / np.sqrt(D_MODEL)
        so = 0.02 / np.sqrt(NUM_HEADS * HEAD_SIZE)
        return {'query': jax.random.normal(ks[0], (B, T, D_MODEL), jnp.float32), 'w_q': jax.random.normal(ks[1], (D_MODEL, NUM_HEADS * HEAD_SIZE), jnp.float32) * s, 'b_q': jnp.zeros((NUM_HEADS * HEAD_SIZE,), jnp.float32), 'w_k': jax.random.normal(ks[2], (D_MODEL, NUM_HEADS * HEAD_SIZE), jnp.float32) * s, 'b_k': jnp.zeros((NUM_HEADS * HEAD_SIZE,), jnp.float32), 'w_v': jax.random.normal(ks[3], (D_MODEL, NUM_HEADS * HEAD_SIZE), jnp.float32) * s, 'b_v': jnp.zeros((NUM_HEADS * HEAD_SIZE,), jnp.float32), 'w_o': jax.random.normal(ks[4], (NUM_HEADS * HEAD_SIZE, MODEL_SIZE), jnp.float32) * so, 'b_o': jnp.zeros((MODEL_SIZE,), jnp.float32)}
    _L0_attn_all = _L0_attn_setup()
    _L0_attn_in = {k: v for k, v in _L0_attn_all.items() if k in ('w_q', 'b_q', 'w_k', 'b_k', 'w_v', 'b_v', 'w_o', 'b_o')}
    del _L0_attn_all

    def _L0_cond2_setup():
        import jax, jax.numpy as jnp
        import numpy as np
        B, T, D = (16, 128, 256)
        key = jax.random.key(seed)
        k0, k1, k2, k3 = jax.random.split(key, 4)
        scale = 1.0 / np.sqrt(D)
        return {'initial_state': jax.random.normal(k0, (B, D), jnp.float32), 'inputs': jax.random.normal(k1, (B, T, D), jnp.float32), 'W_ih': jax.random.normal(k2, (D, 3 * D), jnp.float32) * scale, 'W_hh': jax.random.normal(k3, (D, 3 * D), jnp.float32) * scale, 'b_ih': jnp.zeros((3 * D,), jnp.float32), 'b_hh': jnp.zeros((3 * D,), jnp.float32)}
    _L0_cond2_all = _L0_cond2_setup()
    _L0_cond2_in = {k: v for k, v in _L0_cond2_all.items() if k in ('W_ih', 'W_hh', 'b_ih', 'b_hh')}
    del _L0_cond2_all

    def _L0_ffn_setup():
        import jax, jax.numpy as jnp
        import numpy as np
        B, S, H = (2, 256, 256)
        E, K, F = (32, 4, 176)
        FS = 704
        EPS = 1e-06
        CAP = 128
        key = jax.random.key(seed)
        ks = jax.random.split(key, 10)
        s = 0.02
        return {'hidden_states': jax.random.normal(ks[0], (B, S, H), jnp.float32), 'w_norm': 1.0 + 0.02 * jax.random.normal(ks[1], (H,), jnp.float32), 'w_router': s * jax.random.normal(ks[2], (H, E), jnp.float32), 'w_gate': s * jax.random.normal(ks[3], (E, H, F), jnp.float32), 'w_up': s * jax.random.normal(ks[4], (E, H, F), jnp.float32), 'w_down': s * jax.random.normal(ks[5], (E, F, H), jnp.float32), 'sw_gate': s * jax.random.normal(ks[6], (H, FS), jnp.float32), 'sw_up': s * jax.random.normal(ks[7], (H, FS), jnp.float32), 'sw_down': s * jax.random.normal(ks[8], (FS, H), jnp.float32), 'w_shared_gate': s * jax.random.normal(ks[9], (H, 1), jnp.float32)}
    _L0_ffn_all = _L0_ffn_setup()
    _L0_ffn_in = {k: v for k, v in _L0_ffn_all.items() if k in ('w_norm', 'w_router', 'w_gate', 'w_up', 'w_down', 'sw_gate', 'sw_up', 'sw_down', 'w_shared_gate')}
    del _L0_ffn_all
    return {'x': x, 'cond_2048': cond_2048, 'L0_cond_coupling': _L0_cond_in['coupling'], 'L0_cond_bias': _L0_cond_in['bias'], 'L0_attn_w_q': _L0_attn_in['w_q'], 'L0_attn_b_q': _L0_attn_in['b_q'], 'L0_attn_w_k': _L0_attn_in['w_k'], 'L0_attn_b_k': _L0_attn_in['b_k'], 'L0_attn_w_v': _L0_attn_in['w_v'], 'L0_attn_b_v': _L0_attn_in['b_v'], 'L0_attn_w_o': _L0_attn_in['w_o'], 'L0_attn_b_o': _L0_attn_in['b_o'], 'L0_cond2_W_ih': _L0_cond2_in['W_ih'], 'L0_cond2_W_hh': _L0_cond2_in['W_hh'], 'L0_cond2_b_ih': _L0_cond2_in['b_ih'], 'L0_cond2_b_hh': _L0_cond2_in['b_hh'], 'L0_ffn_w_norm': _L0_ffn_in['w_norm'], 'L0_ffn_w_router': _L0_ffn_in['w_router'], 'L0_ffn_w_gate': _L0_ffn_in['w_gate'], 'L0_ffn_w_up': _L0_ffn_in['w_up'], 'L0_ffn_w_down': _L0_ffn_in['w_down'], 'L0_ffn_sw_gate': _L0_ffn_in['sw_gate'], 'L0_ffn_sw_up': _L0_ffn_in['sw_up'], 'L0_ffn_sw_down': _L0_ffn_in['sw_down'], 'L0_ffn_w_shared_gate': _L0_ffn_in['w_shared_gate']}

def reference(x, cond_2048, L0_cond_coupling, L0_cond_bias, L0_attn_w_q, L0_attn_b_q, L0_attn_w_k, L0_attn_b_k, L0_attn_w_v, L0_attn_b_v, L0_attn_w_o, L0_attn_b_o, L0_cond2_W_ih, L0_cond2_W_hh, L0_cond2_b_ih, L0_cond2_b_hh, L0_ffn_w_norm, L0_ffn_w_router, L0_ffn_w_gate, L0_ffn_w_up, L0_ffn_w_down, L0_ffn_sw_gate, L0_ffn_sw_up, L0_ffn_sw_down, L0_ffn_w_shared_gate):
    import jax
    import jax.numpy as jnp

    def _L0_cond_ref(q0, p0, input_drive_seq, coupling, bias):
        import jax, jax.numpy as jnp
        import numpy as np
        DT = 0.01
        EPSILON = 0.08
        ALPHA = 0.7
        BETA = 0.8
        CLAMP = 20.0
        B, T, N = (32, 128, 256)

        def _derivative(q, p, drive, coupling, bias):
            i_couple = jnp.tanh(q) @ coupling.T
            dq = q - q ** 3 / 3.0 - p + drive + i_couple + bias
            dp = EPSILON * (q + ALPHA - BETA * p)
            return (dq, dp)

        def _rk4_step(q, p, drive, coupling, bias):
            dq1, dp1 = _derivative(q, p, drive, coupling, bias)
            dq2, dp2 = _derivative(q + 0.5 * DT * dq1, p + 0.5 * DT * dp1, drive, coupling, bias)
            dq3, dp3 = _derivative(q + 0.5 * DT * dq2, p + 0.5 * DT * dp2, drive, coupling, bias)
            dq4, dp4 = _derivative(q + DT * dq3, p + DT * dp3, drive, coupling, bias)
            q_next = q + DT / 6.0 * (dq1 + 2 * dq2 + 2 * dq3 + dq4)
            p_next = p + DT / 6.0 * (dp1 + 2 * dp2 + 2 * dp3 + dp4)
            q_next = jnp.clip(q_next, -CLAMP, CLAMP)
            p_next = jnp.clip(p_next, -CLAMP, CLAMP)
            return (q_next, p_next)
        drive_tbn = jnp.swapaxes(input_drive_seq, 0, 1)

        def scan_fn(carry, drive):
            q, p = carry
            q, p = _rk4_step(q, p, drive, coupling, bias)
            return ((q, p), q)
        (_, _), q_trace_tbn = jax.lax.scan(scan_fn, (q0, p0), drive_tbn)
        return jnp.swapaxes(q_trace_tbn, 0, 1)

    def _L0_attn_ref(query, w_q, b_q, w_k, b_k, w_v, b_v, w_o, b_o):
        import jax, jax.numpy as jnp
        import numpy as np
        B, T, D_MODEL = (4, 256, 256)
        NUM_HEADS, HEAD_SIZE = (16, 128)
        MODEL_SIZE = 256
        B_, T_, _ = query.shape
        q = (query @ w_q + b_q).reshape(B_, T_, NUM_HEADS, HEAD_SIZE)
        k = (query @ w_k + b_k).reshape(B_, T_, NUM_HEADS, HEAD_SIZE)
        v = (query @ w_v + b_v).reshape(B_, T_, NUM_HEADS, HEAD_SIZE)
        logits = jnp.einsum('bthd,bThd->bhtT', q, k) * jax.lax.rsqrt(jnp.float32(HEAD_SIZE))
        i = jnp.arange(T_, dtype=jnp.int32)[:, None]
        j = jnp.arange(T_, dtype=jnp.int32)
        mask = (i >= j).astype(logits.dtype)
        logits = logits - 10000000000.0 * (1.0 - mask)
        weights = jax.nn.softmax(logits, axis=-1)
        attn = jnp.einsum('bhtT,bThd->bthd', weights, v).reshape(B_, T_, NUM_HEADS * HEAD_SIZE)
        out = attn @ w_o + b_o
        return out

    def _L0_cond2_ref(initial_state, inputs, W_ih, W_hh, b_ih, b_hh):
        import jax, jax.numpy as jnp
        import numpy as np
        B, T, D = (16, 128, 256)
        "ScanOverTime(GRU cell): sequential per-timestep module call with\n            dict-state passing; merge_dict_trees stacks the per-step\n            'state_predicted' tensors along axis=1 -> [B, T, D]."

        def cell(h, x):
            gi = x @ W_ih + b_ih
            gh = h @ W_hh + b_hh
            i_r, i_z, i_n = jnp.split(gi, 3, axis=-1)
            h_r, h_z, h_n = jnp.split(gh, 3, axis=-1)
            r = jax.nn.sigmoid(i_r + h_r)
            z = jax.nn.sigmoid(i_z + h_z)
            n = jnp.tanh(i_n + r * h_n)
            h_new = (1.0 - z) * n + z * h
            return (h_new, h_new)
        xs = jnp.swapaxes(inputs, 0, 1)
        _, hs = jax.lax.scan(cell, initial_state, xs)
        return jnp.swapaxes(hs, 0, 1)

    def _L0_ffn_ref(hidden_states, w_norm, w_router, w_gate, w_up, w_down, sw_gate, sw_up, sw_down, w_shared_gate):
        import jax, jax.numpy as jnp
        import numpy as np
        B, S, H = (2, 256, 256)
        E, K, F = (32, 4, 176)
        FS = 704
        EPS = 1e-06
        CAP = 128
        inp = hidden_states
        xf = inp.astype(jnp.float32)
        var = jnp.mean(xf * xf, axis=-1, keepdims=True)
        x = (w_norm * (xf * jax.lax.rsqrt(var + EPS))).astype(inp.dtype)
        Bq, Sq, Hq = x.shape
        x = x.reshape(-1, Hq)
        T = Bq * Sq
        logits = x @ w_router
        probs = jax.nn.softmax(logits.astype(jnp.float32), axis=-1)
        w_topk, sel = jax.lax.top_k(probs, K)
        w_topk = w_topk.astype(x.dtype)
        flat_e = sel.reshape(-1)
        order = jnp.argsort(flat_e)
        sorted_e = flat_e[order]
        counts = jnp.zeros((E,), jnp.int32).at[flat_e].add(1)
        starts = jnp.cumsum(counts) - counts
        pos = jnp.arange(T * K) - starts[sorted_e]
        tok = order // K
        valid = pos < CAP
        dest = jnp.where(valid, pos, CAP)
        buf = jnp.zeros((E, CAP + 1, Hq), x.dtype).at[sorted_e, dest].set(x[tok])
        buf = buf[:, :CAP]
        g = jnp.einsum('ech,ehf->ecf', buf, w_gate)
        u = jnp.einsum('ech,ehf->ecf', buf, w_up)
        y = jnp.einsum('ecf,efh->ech', jax.nn.silu(g) * u, w_down)
        wv = w_topk.reshape(-1)[order] * valid.astype(x.dtype)
        gath = y[sorted_e, jnp.minimum(pos, CAP - 1)]
        out = jnp.zeros((T, Hq), x.dtype).at[tok].add(gath * wv[:, None])
        sh = jax.nn.silu(x @ sw_gate) * (x @ sw_up) @ sw_down
        sh = jax.nn.sigmoid(x @ w_shared_gate) * sh
        out = out + sh
        return inp + out.reshape(Bq, Sq, Hq)
    x = x + _L0_attn_ref(_L0_cond_ref(cond_2048, cond_2048, x, L0_cond_coupling, L0_cond_bias), L0_attn_w_q, L0_attn_b_q, L0_attn_w_k, L0_attn_b_k, L0_attn_w_v, L0_attn_b_v, L0_attn_w_o, L0_attn_b_o)
    x = x + _L0_ffn_ref(_L0_cond2_ref(cond_2048, x, L0_cond2_W_ih, L0_cond2_W_hh, L0_cond2_b_ih, L0_cond2_b_hh), L0_ffn_w_norm, L0_ffn_w_router, L0_ffn_w_gate, L0_ffn_w_up, L0_ffn_w_down, L0_ffn_sw_gate, L0_ffn_sw_up, L0_ffn_sw_down, L0_ffn_w_shared_gate)
    return x

_drawn_inputs = setup_inputs


def setup_inputs(seed=0):
    import zlib

    import numpy as np

    out = dict(_drawn_inputs(seed))
    spreads = {'L0_cond_bias': (0.0, 0.8),
     'L0_attn_b_q': (0.0, 0.8),
     'L0_attn_b_k': (0.0, 2.0),
     'L0_attn_b_v': (0.0, 0.8),
     'L0_attn_b_o': (0.0, 0.1),
     'L0_cond2_b_ih': (0.0, 0.1),
     'L0_cond2_b_hh': (0.0, 0.1)}
    factors = {'L0_cond_coupling': 8.0,
     'L0_attn_w_q': 8.0,
     'L0_attn_w_k': 64.0,
     'L0_attn_w_v': 8.0,
     'L0_attn_w_o': 8.0,
     'L0_ffn_w_norm': 8.0,
     'L0_ffn_w_router': 8.0,
     'L0_ffn_w_gate': 8.0,
     'L0_ffn_w_up': 8.0,
     'L0_ffn_w_down': 8.0,
     'L0_ffn_sw_gate': 4.471,
     'L0_ffn_sw_up': 4.421,
     'L0_ffn_sw_down': 4.417,
     'L0_ffn_w_shared_gate': 8.0}
    for name, (base, spread) in spreads.items():
        noise = np.random.default_rng([zlib.crc32(name.encode()), seed]).standard_normal(out[name].shape)
        drawn = base * np.exp(spread * noise) if base else spread * noise
        out[name] = jnp.asarray(drawn.astype(out[name].dtype))
    for name, factor in factors.items():
        out[name] = (out[name] * factor).astype(out[name].dtype)
    return out
```

```python
from contextlib import ExitStack

import numpy as np
import concourse.bass as bass
from concourse import mybir
from concourse.alu_op_type import AluOpType as ALU

F32 = mybir.dt.float32
F16 = mybir.dt.float16
BF16 = mybir.dt.bfloat16
U32 = mybir.dt.uint32
I32 = mybir.dt.int32
ACT = mybir.ActivationFunctionType
AX = mybir.AxisListType

P = 128
B, T, D = 4, 256, 256
DH = D // P
TB = 128
NBLK = T // TB
UNROLL = 16
S8 = DH * B

DT, EPSILON, ALPHA, BETA, CLAMP = 0.01, 0.08, 0.7, 0.8, 20.0
PSHIFT = ALPHA / BETA
PSCALE = EPSILON * BETA
STAGE = [DT / 2, DT / 2, DT]
THIRD = float(np.float32(1 / 3))
THIRD_REST = 1 - 2 * THIRD

NH, HD = 16, 128
SCALE = float(HD) ** -0.5

E, TOPK, F, FS, CAP, NORM_EPS = 32, 4, 176, 704, 128, 1e-6
N = B * T
NT = N // P


def gate_products(nc, m, gates, lo, x, done, opened=False):
    for bank, base, gate in gates:
        for mo in range(DH):
            for k in range(DH):
                for w in ([m.Whh_hi] if lo else [m.Whh_lo, m.Whh_hi]):
                    col = D * gate + P * mo
                    last = nc.tensor.matmul(m.ps[bank][:, base + B * mo:base + B * mo + B],
                                            w[:, k, col:col + P], x[:, B * k:B * k + B],
                                            start=(not lo and not opened and base == 0 and mo == 0 and k == 0 and w is m.Whh_lo),
                                            stop=(lo and mo == 1 and k == 1), skip_group_check=True)
    if lo:
        last.then_inc(done, 1)


def scan_block(nc, m, name, fhn_t0, gru_t0):
    gru = gru_t0 is not None
    sem = lambda what: m.sem(f"{name}_{what}")
    v_ready = sem("v_ready")
    tanh_ready = [sem(f"tanh_ready{h}") for h in range(2)]
    lo_ready = sem("lo_ready")
    couple_done = sem("couple_done")
    gate_done = sem("gate_done")
    gate_pre = sem("gate_pre")
    gate_act = sem("gate_act")
    h_hi_ready = sem("h_hi_ready")
    h_lo_ready = sem("h_lo_ready")
    chain = sem("chain")
    ITERS = TB // UNROLL
    STAGES = 4 * UNROLL
    t_hi = m.t_f[:].bitcast(BF16).rearrange("p (n two) -> p n two", two=2)[:, :, 1]
    half = lambda k: (k % STAGES) // (STAGES // 2)
    tanh_number = lambda k: k % (STAGES // 2) + 1

    with nc.Block() as block:

        @block.scalar
        def _(act):
            act.preload_act_table_set("sigmoid_and_others")

            def tanh(k):
                act.wait_ge(v_ready, k + 1)
                nc.scalar.activation(m.t_f[:], m.U[:, k % 4, 0, :], ACT.Tanh).then_inc(tanh_ready[half(k)], 1)

            with act.Fori(0, ITERS):
                for k in range(STAGES):
                    tanh(k)
                    if gru and k % 4 == 1:
                        act.wait_ge(gate_pre, 2 * (k // 4) + 1)
                        nc.scalar.activation(m.gate[:, 0:2, :], m.gpre[:, 0:2, :], ACT.Sigmoid).then_inc(gate_act, 1)
                    if gru and k % 4 == 3:
                        act.wait_ge(gate_pre, 2 * (k // 4) + 2)
                        nc.scalar.activation(m.gate[:, 2, :], m.gpre[:, 2, :], ACT.Tanh).then_inc(gate_act, 1)
                act.sem_inc(v_ready, -STAGES)
                if gru:
                    act.sem_inc(gate_pre, -2 * UNROLL)
            tanh(0)

        @block.tensor
        def _(pe):
            def coupling(bank, x, lo):
                for mo in range(DH):
                    for k in range(DH):
                        for w in ([m.C_hi] if lo else [m.C_lo, m.C_hi]):
                            last = nc.tensor.matmul(bank[:, B * mo:B * mo + B],
                                                    w[:, k, P * mo:P * mo + P], x[:, B * k:B * k + B],
                                                    start=(not lo and mo == 0 and k == 0 and w is m.C_lo),
                                                    stop=(lo and mo == 1 and k == 1), skip_group_check=True)
                if lo:
                    last.then_inc(couple_done, 1)

            with pe.Fori(0, ITERS):
                for k in range(STAGES):
                    u, s = k // 4, k % 4
                    pe.wait_ge(tanh_ready[half(k)], tanh_number(k))
                    coupling(m.ps[s % 2], t_hi, False)
                    pe.wait_ge(lo_ready, k + 1)
                    coupling(m.ps[s % 2], m.t_lo, True)
                    if gru and s == 0:
                        pe.wait_ge(h_hi_ready, u + 1)
                        gate_products(nc, m, ((4, 0, 0), (4, S8, 1)), False, m.h_hi, None)
                        pe.wait_ge(h_lo_ready, u + 1)
                        gate_products(nc, m, ((4, 0, 0), (4, S8, 1)), True, m.h_lo, gate_done)
                    if gru and s == 1:
                        gate_products(nc, m, ((6, 0, 2),), False, m.h_hi, None)
                        gate_products(nc, m, ((6, 0, 2),), True, m.h_lo, gate_done)
                pe.sem_inc(lo_ready, -STAGES)
                if gru:
                    pe.sem_inc(h_hi_ready, -UNROLL)
                    pe.sem_inc(h_lo_ready, -UNROLL)

        @block.vector
        def _(dve):
            stt, tt, ts = nc.vector.scalar_tensor_tensor, nc.vector.tensor_tensor, nc.vector.tensor_scalar
            count = [0]
            source = [0]

            def step(ins):
                ins.then_inc(chain, 1)
                count[0] += 1
                return count[0]

            def after(n):
                dve.wait_ge(chain, n)

            def fma(out, in0, scalar, in1):
                return stt(out=out, in0=in0, scalar=scalar, in1=in1, op0=ALU.mult, op1=ALU.add)

            def both(row):
                return row.unsqueeze(1).broadcast_to((P, 2, S8))

            def stage(k):
                u, s = k // 4, k % 4
                z, U = m.QP[:, u, :, :], m.U
                Us = z if s == 0 else U[:, s, 0:3:2, :]
                V, p = Us[:, 0, :], Us[:, 1, :]
                a = STAGE[s] if s < 3 else DT / 6
                g, pre, gi = m.gate, m.gpre, m.gi_now[:, u % UNROLL, :]

                if s == 0 and u > 0:
                    after(step(ts(p, m.NX[:, 1, :], (CLAMP - PSHIFT) / PSCALE, (-CLAMP - PSHIFT) / PSCALE,
                                  ALU.min, ALU.max)))
                    clipped = step(ts(V, U[:, 0, 0, :], CLAMP, -CLAMP, ALU.min, ALU.max))
                if s == 0:
                    start = step(fma(m.DR[:], both(p), -a * PSCALE, m.drive_a[:, u, :, :]))
                else:
                    after(source[0])
                    behind = step(fma(m.Y[:] if s == 3 else m.W[:], both(p), -a * PSCALE,
                                      m.S3[:] if s == 3 else m.R[:, s - 1, :, :]))
                    if gru and s == 3:
                        tt(pre[:, 2, :], m.rn[:], gi[:, 2 * S8:3 * S8], ALU.add).then_inc(gate_pre, 1)
                    after(behind)

                def lower_part():
                    dve.wait_ge(tanh_ready[half(k)], tanh_number(k))
                    tt(m.t_lo[:], m.t_f[:], t_hi, ALU.subtract).then_inc(lo_ready, 1)

                if s == 0:
                    lower_part()
                    if u > 0:
                        after(clipped)
                t1 = step(stt(out=m.t1[:, 0, :], in0=V, scalar=-1.0 / 3.0, in1=V, op0=ALU.mult, op1=ALU.mult))
                if s == 0:
                    after(start)
                    step(tt(m.W[:], m.DR[:], z, ALU.add))
                elif s == 1:
                    step(tt(m.S1[:], Us, z, ALU.subtract))
                elif s == 2:
                    sums = step(fma(m.S2[:], Us, 2.0, m.S1[:]))
                else:
                    step(fma(m.W[:], Us, THIRD_REST, m.Y[:]))
                if s > 0:
                    lower_part()
                after(t1)
                t2 = step(stt(out=m.t2[:], in0=m.t1[:], scalar=1.0, in1=both(V), op0=ALU.add, op1=ALU.mult))
                if s == 0:
                    source[0] = step(tt(m.R[:, 0, :, :], m.drive_a[:, u, :, :], z, ALU.add))
                if s == 1:
                    source[0] = step(fma(m.R[:, 1, :, :], m.drive_a[:, u, :, :], 2.0, z))
                if gru and s == 2:
                    dve.wait_ge(gate_done, 2 * u + 2)
                    hn = step(tt(m.hn[:], m.ps[6][:, 0:S8], m.bhn8[:], ALU.add))
                if gru and s == 3:
                    step(tt(m.zh[:], g[:, 1, :], m.H[:, u, :], ALU.mult))
                    dve.wait_ge(gate_act, 2 * u + 2)
                    nz = step(tt(m.nz[:], g[:, 2, :], m.zc[:], ALU.mult))
                after(t2)
                base = step(fma(m.NX[:] if s == 3 else U[:, s + 1, 1:3, :], m.t2[:], a, m.W[:]))
                if gru and s == 2:
                    after(hn)
                    dve.wait_ge(gate_act, 2 * u + 1)
                    step(tt(m.rn[:], m.hn[:], g[:, 0, :], ALU.mult))
                if s == 2:
                    after(sums)
                    source[0] = step(fma(m.S3[:], m.S2[:], THIRD, m.drive_6[:, u, :, :]))
                if gru and s == 0 and u > 0:
                    tt(m.h_lo[:], m.H[:, u, :], m.h_hi[:], ALU.subtract).then_inc(h_lo_ready, 1)
                if gru and s == 1:
                    dve.wait_ge(gate_done, 2 * u + 1)
                    tt(pre[:, 0:2, :].rearrange("p g n -> p (g n)"), m.ps[4][:, 0:2 * S8], gi[:, 0:2 * S8], ALU.add
                       ).then_inc(gate_pre, 1)
                if gru and s == 2:
                    step(ts(m.zc[:], g[:, 1, :], -1.0, 1.0, ALU.mult, ALU.add))
                if gru and s == 3:
                    after(nz)
                    tt(m.h_hi[:], m.nz[:], m.zh[:], ALU.add).then_inc(h_hi_ready, 1)
                    step(tt(m.H[:, u + 1, :], m.nz[:], m.zh[:], ALU.add))
                after(base)

            def next_argument(k):
                u, s = k // 4, k % 4
                dve.wait_ge(couple_done, k + 1)
                if s == 3:
                    fma(m.U[:, 0, 0, :], m.ps[s % 2][:, 0:S8], DT / 6, m.NX[:, 0, :]).then_inc(v_ready, 1)
                else:
                    fma(m.U[:, s + 1, 0, :], m.ps[s % 2][:, 0:S8], STAGE[s], m.U[:, s + 1, 1, :]).then_inc(v_ready, 1)

            dve.sem_inc(v_ready, 1)
            if gru:
                dve.sem_inc(h_hi_ready, 1)
                dve.sem_inc(h_lo_ready, 1)
            drive = m.drive[:, fhn_t0:fhn_t0 + 1, :]
            after(step(ts(m.drive_a[:, 0:1, 0, :], drive, DT / 2, None, ALU.mult)))
            stage(0)
            after(count[0])
            dve.sem_inc(chain, -count[0])
            with dve.Fori(0, ITERS) as i:
                count[0], source[0] = 0, 1
                t = i * UNROLL
                next_argument(0)
                drive = m.drive[:, bass.ds(t + fhn_t0, UNROLL + 1), :]
                step(ts(m.drive_a[:, :, 0, :], drive, DT / 2, None, ALU.mult))
                step(ts(m.drive_6[:, :, 0, :], drive, DT / 6, None, ALU.mult))
                if gru:
                    step(nc.vector.tensor_copy(m.gi_now[:, 0:UNROLL, :], m.gi[:, bass.ds(t, UNROLL), :]))
                for k in range(1, STAGES):
                    stage(k)
                    next_argument(k)
                    if k == STAGES // 2:
                        dve.sem_inc(tanh_ready[0], -STAGES // 2)
                stage(STAGES)
                step(nc.vector.tensor_copy(m.QP[:, 0, :, :], m.QP[:, UNROLL, :, :]))
                step(nc.vector.tensor_copy(m.qT[:, :, :, bass.ds(t + fhn_t0, UNROLL)],
                                           m.QP[:, 1:UNROLL + 1, 0, :].rearrange("p t (h b) -> p h b t", h=DH)))
                dve.sem_inc(tanh_ready[1], -STAGES // 2)
                dve.sem_inc(couple_done, -STAGES)
                if gru:
                    step(nc.vector.tensor_copy(m.hT[:, :, :, bass.ds(t + gru_t0, UNROLL)],
                                               m.H[:, 1:UNROLL + 1, :].rearrange("p t (h b) -> p h b t", h=DH)))
                    step(nc.vector.tensor_copy(m.H[:, 0, :], m.H[:, UNROLL, :]))
                    dve.sem_inc(gate_done, -2 * UNROLL)
                    dve.sem_inc(gate_act, -2 * UNROLL)
                after(count[0])
                dve.sem_inc(chain, -count[0])


def gru_block(nc, m, name, gru_t0):
    sem = lambda what: m.sem(f"{name}_{what}")
    h_hi_ready = sem("h_hi_ready")
    h_lo_ready = sem("h_lo_ready")
    gi_ready = sem("gi_ready")
    rz_done = sem("rz_done")
    n_done = sem("n_done")
    n_pre = sem("n_pre")
    gate_act = sem("gate_act")
    chain = sem("chain")
    bank = lambda u, g: 2 + 3 * (u % 2) + g

    with nc.Block() as block:

        @block.scalar
        def _(act):
            act.preload_act_table_set("sigmoid_and_others")
            with act.Fori(0, TB // UNROLL):
                for u in range(UNROLL):
                    for g in range(2):
                        act.wait_ge(rz_done, 2 * u + g + 1)
                        nc.scalar.activation(m.gate[:, g, :], m.ps[bank(u, g)][:, 0:S8], ACT.Sigmoid).then_inc(gate_act, 1)
                    act.wait_ge(n_pre, u + 1)
                    nc.scalar.activation(m.gate[:, 2, :], m.gpre[:, 2, :], ACT.Tanh).then_inc(gate_act, 1)
                act.sem_inc(rz_done, -2 * UNROLL)
                act.sem_inc(n_pre, -UNROLL)

        @block.tensor
        def _(pe):
            def open_rz(u):
                for g in range(2):
                    nc.tensor.matmul(m.ps[bank(u, g)][:, 0:S8], m.ident[:], m.gi_now[:, u, S8 * g:S8 * g + S8],
                                     start=True, stop=False, skip_group_check=True)

            pe.wait_ge(gi_ready, 1)
            open_rz(0)
            with pe.Fori(0, TB // UNROLL):
                for u in range(UNROLL):
                    r, z, n = ((bank(u, g), 0, g) for g in range(3))
                    pe.wait_ge(h_hi_ready, u + 1)
                    gate_products(nc, m, (r,), False, m.h_hi, None, opened=True)
                    gate_products(nc, m, (n,), False, m.h_hi, None)
                    pe.wait_ge(h_lo_ready, u + 1)
                    gate_products(nc, m, (r,), True, m.h_lo, rz_done)
                    gate_products(nc, m, (n,), True, m.h_lo, n_done)
                    gate_products(nc, m, (z,), False, m.h_hi, None, opened=True)
                    gate_products(nc, m, (z,), True, m.h_lo, rz_done)
                    if u == 0:
                        pe.wait_ge(gi_ready, 2)
                    open_rz(u + 1)
                pe.sem_inc(h_hi_ready, -UNROLL)
                pe.sem_inc(h_lo_ready, -UNROLL)
                pe.sem_inc(gi_ready, -1)

        @block.vector
        def _(dve):
            tt, ts = nc.vector.tensor_tensor, nc.vector.tensor_scalar
            count = [0]

            def step(ins):
                ins.then_inc(chain, 1)
                count[0] += 1
                return count[0]

            def after(n):
                dve.wait_ge(chain, n)

            nc.vector.tensor_copy(m.gi_now[:, 0:1, :], m.gi[:, 0:1, :]).then_inc(gi_ready, 1)
            dve.sem_inc(h_hi_ready, 1)
            dve.sem_inc(h_lo_ready, 1)
            with dve.Fori(0, TB // UNROLL) as i:
                count[0] = 0
                t = i * UNROLL
                for u in range(UNROLL):
                    g, pre, gi = m.gate, m.gpre, m.gi_now[:, u, :]
                    dve.wait_ge(n_done, u + 1)
                    hn = step(tt(m.hn[:], m.ps[bank(u, 2)][:, 0:S8], m.bhn8[:], ALU.add))
                    if u == 0:
                        nc.vector.tensor_copy(m.gi_now[:], m.gi[:, bass.ds(t, UNROLL + 1), :]).then_inc(gi_ready, 1)
                    dve.wait_ge(gate_act, 3 * u + 1)
                    after(hn)
                    after(step(tt(m.rn[:], m.hn[:], g[:, 0, :], ALU.mult)))
                    tt(pre[:, 2, :], m.rn[:], gi[:, 2 * S8:3 * S8], ALU.add).then_inc(n_pre, 1)
                    dve.wait_ge(gate_act, 3 * u + 2)
                    step(ts(m.zc[:], g[:, 1, :], -1.0, 1.0, ALU.mult, ALU.add))
                    zh = step(tt(m.zh[:], g[:, 1, :], m.H[:, u, :], ALU.mult))
                    after(zh)
                    dve.wait_ge(gate_act, 3 * u + 3)
                    after(step(tt(m.nz[:], g[:, 2, :], m.zc[:], ALU.mult)))
                    tt(m.h_hi[:], m.nz[:], m.zh[:], ALU.add).then_inc(h_hi_ready, 1)
                    after(step(tt(m.H[:, u + 1, :], m.nz[:], m.zh[:], ALU.add)))
                    tt(m.h_lo[:], m.H[:, u + 1, :], m.h_hi[:], ALU.subtract).then_inc(h_lo_ready, 1)
                step(nc.vector.tensor_copy(m.hT[:, :, :, bass.ds(t + gru_t0, UNROLL)],
                                           m.H[:, 1:UNROLL + 1, :].rearrange("p t (h b) -> p h b t", h=DH)))
                step(nc.vector.tensor_copy(m.H[:, 0, :], m.H[:, UNROLL, :]))
                dve.sem_inc(n_done, -UNROLL)
                dve.sem_inc(gate_act, -3 * UNROLL)
                after(count[0])
                dve.sem_inc(chain, -count[0])


def attention_block(nc, m, a, kv, blk):
    NK = blk + 1
    KW = NK * TB
    HB = B // 2
    time = slice(blk * TB, blk * TB + TB)
    name = f"a{blk}"
    sem = lambda what: m.sem(f"{name}_{what}")
    w_loaded = [sem(f"w_loaded{i}") for i in range(2)]
    kv_stored = [sem(f"kv_stored{i}") for i in range(2)]
    k_loaded = [sem(f"k_loaded{i}") for i in range(2)]
    v_loaded = [sem(f"v_loaded{i}") for i in range(2)]
    qkv_mm = sem("qkv_mm")
    qkv_sb = sem("qkv_sb")
    s_mm = sem("s_mm")
    l_sb = sem("l_sb")
    nmax = sem("nmax")
    exps = sem("exps")
    rsum = sem("rsum")
    p_ready = sem("p_ready")
    t_mm = sem("t_mm")
    pt_sb = sem("pt_sb")
    pv_mm = sem("pv_mm")
    at_sb = sem("at_sb")
    chain = sem("chain")
    proj_mm, x2_ready, gi_mm, gi_free = sem("proj_mm"), sem("x2_ready"), sem("gi_mm"), sem("gi_free")
    psQ, psK, psV = m.ps[0], m.ps[1], m.ps[2]
    psS, psT, psA = m.ps[3:5], m.ps[5:7], m.ps[7]
    PAIRS = NH // 2

    with nc.Block() as block:

        @block.sync
        def _(sp):
            row = lambda x: x.rearrange("o p n -> p (o n)")
            KV = B * TB

            def load_w(g, par):
                sp.dma_start(m.wbuf[par][:], row(a["wqkv"][bass.ds(g, 1), :, :])).then_inc(w_loaded[par], 16)

            def load_k(g, par):
                sp.dma_start(m.kvold[par][:, 0:KV], row(kv[bass.ds(g, 1), :, 0:KV])).then_inc(k_loaded[par], 16)

            def load_v(g, par):
                sp.dma_start(m.kvold[par][:, KV:2 * KV], row(kv[bass.ds(g, 1), :, KV:2 * KV])).then_inc(v_loaded[par], 16)

            def store(g, par):
                sp.wait_ge(qkv_sb, g * 3 + 3)
                sp.dma_start(row(kv[bass.ds(g, 1), :, :]), m.kvnew[par][:]).then_inc(kv_stored[par], 16)

            for par in range(2):
                load_w(par, par)
            if blk:
                for par in range(2):
                    load_k(par, par)
                    load_v(par, par)
            with sp.Fori(0, PAIRS - 1) as i:
                for par in range(2):
                    g = i * 2 + par
                    if blk:
                        sp.wait_ge(qkv_sb, g * 3 + 3)
                        load_w(g + 2, par)
                        sp.wait_ge(s_mm, g * 2 + 2)
                        load_k(g + 2, par)
                        sp.wait_ge(pv_mm, g + 1)
                        load_v(g + 2, par)
                    else:
                        store(g, par)
                        load_w(g + 2, par)
            if not blk:
                for par in range(2):
                    store(NH - 2 + par, par)
                for par in range(2):
                    sp.wait_ge(kv_stored[par], 16 * (PAIRS + 1))

        @block.tensor
        def _(pe):
            mm = nc.tensor.matmul

            def project_qk(g, par, loads):
                w = m.wbuf[par][:, 0:3 * DH * HD].rearrange("p (c k n) -> p c k n", c=3, k=DH)
                pe.wait_ge(w_loaded[par], loads)
                for c, bank in ((0, psQ), (1, psK)):
                    for k in range(DH):
                        last = mm(bank[:, 0:B * TB], w[:, c, k, :], m.qT[:, k, :, time], start=(k == 0), stop=(k == DH - 1))
                    last.then_inc(qkv_mm, 1)

            def project_v(par):
                w = m.wbuf[par][:, 0:3 * DH * HD].rearrange("p (c k n) -> p c k n", c=3, k=DH)
                for b in range(B):
                    for k in range(DH):
                        last = mm(psV[:, b * HD:b * HD + HD], m.qT[:, k, b, time], w[:, 2, k, :],
                                  start=(k == 0), stop=(k == DH - 1))
                last.then_inc(qkv_mm, 1)

            def logits(g, par, loads):
                q, kn = m.qnew[par], m.kvnew[par]
                pe.wait_ge(qkv_sb, g * 3 + 3)
                pe.wait_ge(l_sb, g * 2 + 2)
                if blk:
                    pe.wait_ge(k_loaded[par], loads)
                for b in range(B):
                    o = (b % HB) * KW
                    cols = slice(b * TB, b * TB + TB)
                    if blk:
                        mm(psS[b // HB][:, o:o + TB], q[:, cols], m.kvold[par][:, cols], start=True, stop=True)
                        o += TB
                    last = mm(psS[b // HB][:, o:o + TB], q[:, cols], kn[:, cols], start=True, stop=True)
                    if b % HB == HB - 1:
                        last.then_inc(s_mm, 1)

            def transpose_p(g, par):
                for b in range(B):
                    pe.wait_ge(p_ready, g * 4 + (b + 1))
                    for k in range(NK):
                        o = ((b % HB) * NK + k) * TB
                        last = nc.tensor.transpose(psT[b // HB][:, o:o + TB], m.prob[par][:, b, k * TB:k * TB + TB], m.ident[:])
                    if b % HB == HB - 1:
                        last.then_inc(t_mm, 1)

            def weigh_v(g, par, loads):
                pe.wait_ge(at_sb, g + 1)
                if blk:
                    pe.wait_ge(v_loaded[par], loads)
                for b in range(B):
                    if b % HB == 0:
                        pe.wait_ge(pt_sb, g * 2 + (b // HB + 1))
                    cols = slice(b * HD, b * HD + HD)
                    for k in range(NK):
                        v = m.kvnew[par][:, B * TB:] if k == blk else m.kvold[par][:, B * TB:]
                        last = mm(psA[:, b * TB:b * TB + TB], v[:, cols], m.probT[:, b, k * TB:k * TB + TB],
                                  start=(k == 0), stop=(k == NK - 1))
                last.then_inc(pv_mm, 1)

            project_qk(0, 0, 16)
            project_v(0)
            logits(0, 0, 16)
            project_qk(1, 1, 16)
            project_v(1)
            with pe.Fori(0, PAIRS - 1) as i:
                for par in (1, 0):
                    g = i * 2 + (2 - par)
                    logits(g, par, i * 16 + (32 - 16 * par))
                    transpose_p(g + (-1), 1 - par)
                    project_qk(g + 1, 1 - par, i * 16 + 32)
                    weigh_v(g + (-1), 1 - par, i * 16 + 16)
                    project_v(1 - par)
            logits(NH - 1, 1, 16 * PAIRS)
            for par in range(2):
                transpose_p(NH - 2 + par, par)
                weigh_v(NH - 2 + par, par, 16 * PAIRS)
            pe.wait_ge(at_sb, NH + 1)
            pe.wait_ge(m.wo_loaded, 32)
            for mo in range(DH):
                for h in range(NH):
                    last = mm(m.ps[mo][:, 0:B * TB], m.wo[:, h, mo * P:mo * P + P], m.atT[:, h, :],
                              start=(h == 0), stop=(h == NH - 1))
                last.then_inc(proj_mm, 1)
            pe.wait_ge(x2_ready, DH)
            for c in range(6):
                for k in range(DH):
                    last = mm(m.ps[2 + c][:, 0:B * TB], m.Wih[:, k, c * P:c * P + P], m.x2T[:, k, :, time],
                              start=(k == 0), stop=(k == DH - 1))
                last.then_inc(gi_mm, 1)

        @block.scalar
        def _(act):
            act.preload_act_table_set("exp_and_others")
            act.sem_inc(at_sb, 1)
            if not blk:
                for par in range(2):
                    act.sem_inc(kv_stored[par], 16)

            def evacuate_qk(g, par, stores):
                bias = m.wbuf[par][:, 3 * DH * HD:]
                if not blk:
                    act.wait_ge(kv_stored[par], stores)
                act.wait_ge(qkv_mm, g * 3 + 1)
                nc.scalar.activation(m.qnew[par][:], psQ[:, 0:B * TB], ACT.Identity, bias=bias[:, 0:1]).then_inc(qkv_sb, 1)
                act.wait_ge(qkv_mm, g * 3 + 2)
                nc.scalar.activation(m.kvnew[par][:, 0:B * TB], psK[:, 0:B * TB], ACT.Identity, bias=bias[:, 1:2]).then_inc(qkv_sb, 1)

            def evacuate_v(g, par, first=False):
                act.wait_ge(qkv_mm, g * 3 + 3)
                nc.scalar.activation(m.kvnew[par][:, B * TB:], psV[:, 0:B * HD], ACT.Identity)
                if not first:
                    act.wait_ge(at_sb, g)
                nc.scalar.activation(m.vbias[:, par:par + 1], m.wbuf[par][:, 3 * DH * HD + 2:], ACT.Identity).then_inc(qkv_sb, 1)

            def exponents(g, par):
                act.wait_ge(nmax, g + 1)
                for b in range(B):
                    nc.scalar.activation(m.prob[par][:, b, 0:KW], m.logit[:, b, 0:KW], ACT.Exp, bias=m.nmax[:, b:b + 1],
                                         accum_out=m.psum_[:, par, b:b + 1]).then_inc(exps, 1)

            def result(g, par):
                act.wait_ge(qkv_sb, g * 3 + 3)
                act.wait_ge(pv_mm, g + 1)
                nc.scalar.activation(m.atT[:, bass.ds(g, 1), :].rearrange("p o n -> p (o n)"), psA[:, 0:B * TB], ACT.Identity,
                                     bias=m.vbias[:, par:par + 1]).then_inc(at_sb, 1)

            def evacuate(g, par):
                act.wait_ge(w_loaded[par], 16)
                evacuate_qk(g, par, 16)
                evacuate_v(g, par, first=g == 0)

            evacuate(0, 0)
            exponents(0, 0)
            evacuate(1, 1)
            act.wait_ge(m.x_zeroed, 16 * 4)
            with act.Fori(0, PAIRS - 1) as i:
                for par in (1, 0):
                    g = i * 2 + (2 - par)
                    exponents(g, par)
                    act.wait_ge(w_loaded[1 - par], i * 16 + 32)
                    evacuate_qk(g + 1, 1 - par, i * 16 + 32)
                    result(g + (-1), 1 - par)
                    evacuate_v(g + 1, 1 - par)
            exponents(NH - 1, 1)
            result(NH - 2, 0)
            result(NH - 1, 1)
            for c in range(6):
                act.wait_ge(gi_mm, c + 1)
                last = nc.scalar.activation(m.gi[:, 0:TB, c * B:c * B + B].rearrange("p t b -> p b t"),
                                            m.ps[2 + c][:, 0:B * TB].rearrange("p (b t) -> p b t", b=B),
                                            ACT.Identity, bias=m.bgi[:, c:c + 1])

        @block.gpsimd
        def _(pool):
            with pool.Fori(0, PAIRS):
                for par in range(2):
                    pool.wait_ge(rsum, par + 1)
                    for b in range(B):
                        pr = m.prob[par][:, b, 0:KW]
                        nc.gpsimd.tensor_scalar(pr, pr, m.rsum[:, par, b:b + 1], None, ALU.mult).then_inc(p_ready, 1)
                pool.sem_inc(rsum, -2)

        @block.vector
        def _(dve):
            v = nc.vector
            dve.sem_inc(l_sb, 2)
            if not blk:
                prepare_gru(nc, m, dve)

            def maxima(g):
                for half in range(2):
                    dve.wait_ge(s_mm, g * 2 + (half + 1))
                    v.scalar_tensor_tensor(out=m.logit[:, half * HB:half * HB + HB, 0:KW],
                                           in0=psS[half][:, 0:HB * KW].rearrange("p (b k) -> p b k", b=HB), scalar=SCALE,
                                           in1=m.mask[:, 0:HB, T - KW:T], op0=ALU.mult, op1=ALU.add).then_inc(l_sb, 1)
                dve.wait_ge(l_sb, g * 2 + 4)
                v.tensor_reduce(m.nmax[:], m.logit[:, :, 0:KW], AX.X, ALU.max, negate=True).then_inc(nmax, 1)

            def transposed_p(g):
                for half in range(2):
                    dve.wait_ge(t_mm, g * 2 + (half + 1))
                    v.tensor_copy(m.probT[:, half * HB:half * HB + HB, 0:KW],
                                  psT[half][:, 0:HB * KW].rearrange("p (b k) -> p b k", b=HB)).then_inc(pt_sb, 1)

            def sums(g, par):
                dve.wait_ge(exps, g * 4 + 4)
                v.reciprocal(m.rsum[:, par, :], m.psum_[:, par, :]).then_inc(rsum, 1)

            maxima(0)
            sums(0, 0)
            with dve.Fori(0, PAIRS - 1) as i:
                for par in (1, 0):
                    g = i * 2 + (2 - par)
                    maxima(g)
                    transposed_p(g + (-1))
                    sums(g, par)
            maxima(NH - 1)
            transposed_p(NH - 2)
            sums(NH - 1, 1)
            transposed_p(NH - 1)
            for mo in range(DH):
                dve.wait_ge(proj_mm, mo + 1)
                v.scalar_tensor_tensor(out=m.x2T[:, mo, :, time],
                                       in0=m.ps[mo][:, 0:B * TB].rearrange("p (b t) -> p b t", b=B), scalar=m.bo[:, mo:mo + 1],
                                       in1=m.x[:, time, B * mo:B * mo + B].rearrange("p t b -> p b t"),
                                       op0=ALU.add, op1=ALU.add).then_inc(x2_ready, 1)


class Memory:

    def __init__(self, nc, ctx):
        self.nc, self.ctx = nc, ctx

    def sem(self, name):
        return self.ctx.enter_context(self.nc.semaphore(name))

    def sb(self, name, shape, dt=F32):
        return self.ctx.enter_context(self.nc.sbuf_tensor(name, shape, dt))


def allocate_scans(m):
    m.ps = [m.ctx.enter_context(m.nc.psum_tensor(f"bank{i}", [P, 512], F32)) for i in range(8)]
    m.ident = m.sb("ident", [P, P])
    m.x = m.sb("x_steps", [P, T, S8])
    m.drive = m.sb("drive", [P, T + 1, S8])
    m.qT = m.sb("qT", [P, DH, B, T])
    m.x2T = m.sb("x2T", [P, DH, B, T])
    m.hT = m.sb("hT", [P, DH, B, T])
    m.C_hi, m.C_lo = m.sb("C_hi", [P, DH, D], F16), m.sb("C_lo", [P, DH, D], BF16)
    m.Whh_hi, m.Whh_lo = m.sb("Whh_hi", [P, DH, 3 * D], F16), m.sb("Whh_lo", [P, DH, 3 * D], BF16)
    m.Wih = m.sb("Wih", [P, DH, 3 * D])
    m.gi = m.sb("gi", [P, TB + 1, 3 * S8])
    m.U = m.sb("U", [P, 4, 3, S8])
    m.QP = m.sb("QP", [P, UNROLL + 1, 2, S8])
    m.H = m.sb("H", [P, UNROLL + 1, S8])
    m.gi_now = m.sb("gi_now", [P, UNROLL + 1, 3 * S8])
    m.drive_a = m.sb("drive_a", [P, UNROLL + 1, 2, S8])
    m.drive_6 = m.sb("drive_6", [P, UNROLL + 1, 2, S8])
    m.t_f, m.t_lo = m.sb("t_f", [P, S8]), m.sb("t_lo", [P, S8], F16)
    m.R = m.sb("R", [P, 2, 2, S8])
    m.t1 = m.sb("t1", [P, 2, S8])
    m.t2, m.W, m.DR, m.Y, m.NX, m.S1, m.S2, m.S3 = (m.sb(f"pair_{n}", [P, 2, S8]) for n in range(8))
    m.zc, m.zh, m.nz, m.hn, m.rn, m.bhn8 = (m.sb(f"gru_{n}", [P, S8]) for n in range(6))
    m.h_hi, m.h_lo = m.sb("h_hi", [P, S8], F16), m.sb("h_lo", [P, S8], BF16)
    m.gpre, m.gate = m.sb("gpre", [P, 3, S8]), m.sb("gate", [P, 3, S8])
    m.bih, m.bhh = m.sb("bih", [P, 6]), m.sb("bhh", [P, 6])
    m.bgi = m.sb("bgi", [P, 6])


def allocate_attention(m):
    two = lambda n, shape: [m.sb(f"{n}{i}", shape) for i in range(2)]
    m.wbuf = two("wbuf", [P, 3 * DH * HD + 3])
    m.kvold, m.kvnew = two("kvold", [P, 2 * B * TB]), two("kvnew", [P, 2 * B * TB])
    m.qnew = two("qnew", [P, B * TB])
    m.prob = two("prob", [P, B, T])
    m.logit, m.probT = m.sb("logit", [P, B, T]), m.sb("probT", [P, B, T])
    m.atT = m.sb("atT", [P, NH, B * TB])
    m.wo = m.sb("wo", [P, NH, D])
    m.mask = m.sb("mask", [P, B // 2, T])
    m.nmax, m.psum_, m.rsum = m.sb("nmax", [P, B]), m.sb("psum_", [P, 2, B]), m.sb("rsum", [P, 2, B])
    m.bo = m.sb("bo", [P, DH])
    m.vbias = m.sb("vbias", [P, 2])
    m.wo_loaded = m.sem("wo_loaded")
    m.x_zeroed = m.sem("x_zeroed")


def prepare_gru(nc, m, dve):
    v, n = nc.vector, [0]

    def step(ins):
        ins.then_inc(m.gru_prepared, 1)
        n[0] += 1

    dve.wait_ge(m.gru_loaded, 16 * 4)
    step(v.tensor_copy(m.Whh_hi[:], m.stage_w[:]))
    step(v.tensor_copy(m.H[:, 0, :], m.cond[:]))
    step(v.tensor_copy(m.h_hi[:], m.cond[:]))
    step(v.tensor_copy(m.bgi[:, 4:6], m.bih[:, 4:6]))
    step(v.tensor_tensor(m.bgi[:, 0:4], m.bih[:, 0:4], m.bhh[:, 0:4], ALU.add))
    step(v.memset(m.gi[:, TB:TB + 1, :], 0.0))
    for h in range(DH):
        cols = slice(B * h, B * h + B)
        step(v.tensor_scalar(m.bhn8[:, cols], m.cond[:, cols], 0.0, m.bhh[:, 4 + h:5 + h], ALU.mult, ALU.add))
    dve.wait_ge(m.gru_prepared, n[0])
    step(v.tensor_tensor(m.Whh_lo[:], m.stage_w[:], m.Whh_hi[:], ALU.subtract))
    step(v.tensor_tensor(m.h_lo[:], m.H[:, 0, :], m.h_hi[:], ALU.subtract))
    dve.wait_ge(m.gru_prepared, n[0])


def setup(nc, m, a, xbuf):
    load = m.sem("setup_load")
    m.stage_w = m.sb("stage_w", [P, DH, 3 * D])
    stage_c = m.sb("stage_c", [P, DH, D])
    m.cond, bias = m.sb("cond", [P, S8]), m.sb("bias", [P, DH])
    cond = m.cond
    bshift = m.sb("bshift", [P, DH])
    zeros_ready = m.sem("setup_zeros")
    m.gru_loaded, m.gru_prepared = m.sem("gru_loaded"), m.sem("gru_prepared")
    done, ident0 = m.sem("setup_done"), m.sem("setup_ident")
    LOADS = ((stage_c, "couple"), (cond, "cond"), (bias, "bias"), (m.x, "x"))
    GRU_LOADS = ((m.stage_w, "whh"), (m.bhh, "bhh"), (m.bih, "bih"), (m.Wih, "wih"))
    with nc.Block() as block:

        @block.sync
        def _(sp):
            for dst, name in LOADS:
                sp.dma_start(dst[:], a[name]).then_inc(load, 16)
            for dst, name in GRU_LOADS:
                sp.dma_start(dst[:], a[name]).then_inc(m.gru_loaded, 16)
            sp.dma_start(m.bo[:], a["bo"]).then_inc(m.wo_loaded, 16)
            sp.dma_start(m.wo[:], a["wo"]).then_inc(m.wo_loaded, 16)
            sp.wait_ge(zeros_ready, 1)
            rows = xbuf[0:E * CAP, :].rearrange("(q p r) d -> q p (r d)", q=4, p=P)
            for q in range(4):
                sp.dma_start(rows[q], m.atT[:, 0:4, :].rearrange("p h n -> p (h n)")).then_inc(m.x_zeroed, 16)

        @block.gpsimd
        def _(pool):
            nc.gpsimd.memset(m.ident[:], 0.0).then_inc(ident0, 1)
            pool.wait_ge(ident0, 1)
            nc.gpsimd.affine_select(out=m.ident[:], in_=m.ident[:], compare_op=ALU.not_equal, fill=1.0, base=0,
                                    pattern=[[-1, P]], channel_multiplier=1).then_inc(ident0, 1)
            nc.gpsimd.memset(m.atT[:, 0:4, :], 0.0).then_inc(zeros_ready, 1)
            nc.gpsimd.memset(m.mask[:], 0.0).then_inc(ident0, 1)
            pool.wait_ge(ident0, 3)
            nc.gpsimd.affine_select(out=m.mask[:, :, T - TB:T], in_=m.mask[:, :, T - TB:T], compare_op=ALU.is_ge,
                                    fill=-1e10, base=0, pattern=[[0, B // 2], [-1, TB]], channel_multiplier=1
                                    ).then_inc(ident0, 1)

        @block.vector
        def _(dve):
            v, n = nc.vector, [0]

            def step(ins):
                ins.then_inc(done, 1)
                n[0] += 1

            dve.wait_ge(load, 16 * len(LOADS))
            step(v.tensor_copy(m.C_hi[:], stage_c[:]))
            step(v.tensor_copy(m.U[:, 0, 0, :], cond[:]))
            step(v.tensor_copy(m.QP[:, 0, 0, :], cond[:]))
            step(v.tensor_scalar(m.QP[:, 0, 1, :], cond[:], -PSHIFT, 1.0 / PSCALE, ALU.add, ALU.mult))
            step(v.memset(m.t1[:, 1, :], 1.0 / BETA - 1.0))
            step(v.memset(m.drive[:, T:T + 1, :], 0.0))
            step(v.memset(m.drive_a[:, :, 1, :], 0.0))
            step(v.memset(m.drive_6[:, :, 1, :], 0.0))
            step(v.tensor_scalar(bshift[:], bias[:], -PSHIFT, None, ALU.add))
            dve.wait_ge(done, n[0])
            step(v.tensor_tensor(m.C_lo[:], stage_c[:], m.C_hi[:], ALU.subtract))
            for h in range(DH):
                cols = slice(B * h, B * h + B)
                step(v.tensor_scalar(m.drive[:, 0:T, cols], m.x[:, :, cols], bshift[:, h:h + 1], None, ALU.add))
            dve.wait_ge(done, n[0])


FC = [P] * (FS // P) + ([FS % P] if FS % P else [])
FH = F // 2
TRASH = E * CAP


def allocate_moe(m):
    sb = m.sb
    m.h_tok, m.xn = sb("h_tok", [P, NT, D]), sb("xn", [P, NT, D])
    m.xnT = sb("xnT", [P, DH, N])
    m.acc = sb("acc", [P, NT, D])
    m.resT = sb("resT", [P, DH, N])
    m.sq = sb("sq", [P, D])
    m.wn = sb("wn", [P, D])
    m.ss, m.var, m.root, m.rstd, m.newt, m.lmax, m.lsum, m.linv, m.gate_s = (sb(f"token_{n}", [P, NT]) for n in range(9))
    m.wr = sb("wr", [P, DH, E + 1])
    m.logits = sb("logits", [P, NT, E + 1])
    m.probs = sb("probs", [P, NT, E])
    m.top8, m.idx8 = sb("top8", [P, NT, 8]), sb("idx8", [P, NT, 8], U32)
    m.idxf = sb("idxf", [P, NT, TOPK])
    m.lanes_i, m.lanes = sb("lanes_i", [P, E], I32), sb("lanes", [P, E])
    m.flat_i, m.flat = sb("flat_i", [P, NT, TOPK], I32), sb("flat", [P, NT, TOPK])
    m.hot, m.hotpos = sb("hot", [P, NT, TOPK, E]), sb("hotpos", [P, NT, TOPK, E])
    m.picked_f = sb("picked_f", [P, NT, E])
    m.picked = sb("picked", [P, NT, E], BF16)
    m.before, m.ones = sb("before", [P, P], BF16), sb("ones", [P, P], BF16)
    m.posk, m.valid, m.slot, m.wk = (sb(n, [P, NT, TOPK]) for n in ("posk", "valid", "slot", "wk"))
    m.dest_f, m.from_f = sb("dest_f", [P, NT, TOPK]), sb("from_f", [P, NT, TOPK])
    m.dest, m.frm = sb("dest", [P, NT * TOPK], I32), sb("frm", [P, NT * TOPK], I32)
    m.swg, m.swu = sb("swg", [P, DH, FS]), sb("swu", [P, DH, FS])
    m.swd = sb("swd", [P, len(FC), D])
    m.ssig, m.sgate = [sb(f"ssig{i}", [P, 512]) for i in range(2)], sb("sgate", [P, 512])
    m.shT = sb("shT", [P, len(FC), N])
    m.xe = [sb(f"xe{i}", [P, D]) for i in range(2)]
    m.xeT = [sb(f"xeT{i}", [P, DH, CAP]) for i in range(2)]
    m.wgu = [sb(f"wgu{i}", [P, DH, 2 * F]) for i in range(2)]
    m.wdn = [sb(f"wdn{i}", [FH, 2, D]) for i in range(2)]
    m.esig = [sb(f"esig{i}", [P, F]) for i in range(2)]
    m.eg, m.eh = sb("eg", [P, F]), sb("eh", [P, F])
    m.ehT = sb("ehT", [FH, 2, CAP])
    m.y = [sb(f"y{i}", [P, D]) for i in range(2)]
    m.got = [sb(f"got{i}", [P, TOPK, D]) for i in range(2)]


def moe(nc, m, a, xbuf, ybuf, out):
    sem = lambda what: m.sem(f"m_{what}")
    loaded, consts = sem("loaded"), sem("consts")
    gu_loaded = [sem(f"gu_loaded{i}") for i in range(2)]
    dn_loaded = [sem(f"dn_loaded{i}") for i in range(2)]
    x_loaded = [sem(f"x_loaded{i}") for i in range(2)]
    y_stored = [sem(f"y_stored{i}") for i in range(2)]
    hT_mm, h_sb, ss_done = sem("hT_mm"), sem("h_sb"), sem("ss_done")
    chain = sem("chain")
    var_ready, root_ready, xn_ready = sem("var_ready"), sem("root_ready"), sem("xn_ready")
    xnT_mm, xnT_sb, rt_mm = sem("xnT_mm"), sem("xnT_sb"), sem("rt_mm")
    lsub_ready, lexp_ready, picked_ready, pos_mm = sem("lsub_ready"), sem("lexp_ready"), sem("picked_ready"), sem("pos_mm")
    dest_ready, scattered = sem("dest_ready"), sem("scattered")
    sh_mm, sh_sig, sh_h = sem("sh_mm"), sem("sh_sig"), sem("sh_h")
    res_ready, res_mm, res_sb, shd_mm, acc_ready = sem("res_ready"), sem("res_mm"), sem("res_sb"), sem("shd_mm"), sem("acc_ready")
    xeT_mm, xeT_sb, gu_mm, sig_sb, eh_sb, ehT_mm, ehT_sb, y_mm, y_sb = (
        sem(n) for n in ("xeT_mm", "xeT_sb", "gu_mm", "sig_sb", "eh_sb", "ehT_mm", "ehT_sb", "y_mm", "y_sb"))
    gathered = [sem(f"gathered{i}") for i in range(2)]
    acc_done, stored, echain = sem("acc_done"), sem("stored"), sem("echain")
    LOADS = ((m.wn, "wn"), (m.wr, "wr"), (m.swg, "swg"), (m.swu, "swu"))
    EP = E // 2
    STEPS = [(c, half) for c in range(len(FC)) for half in range(2)]
    tile_of = lambda src, i: src[:, :, i * P:(i + 1) * P]
    hT = m.hT[:].rearrange("p h b t -> p h (b t)")
    x2T = m.x2T[:].rearrange("p h b t -> p h (b t)")

    with nc.Block() as block:

        @block.sync
        def _(sp):
            for dst, name in LOADS:
                sp.dma_start(dst[:], a[name]).then_inc(loaded, 16)
            for c, n in enumerate(FC):
                sp.dma_start(m.swd[0:n, c, :], a["swd"][c * P:c * P + n, :]).then_inc(loaded, 16)

            whole = lambda x: x.rearrange("o p n -> p (o n)").rearrange("p (k n) -> p k n", k=2)

            def load_gate_up(e, par):
                sp.dma_start(m.wgu[par][:], whole(a["wgu"][bass.ds(e, 1), :, :])).then_inc(gu_loaded[par], 16)

            def load_down(e, par):
                sp.dma_start(m.wdn[par][:], whole(a["wdn"][bass.ds(e, 1), :, :])).then_inc(dn_loaded[par], 16)

            def load_x(e, par):
                sp.dma_start(m.xe[par][:], xbuf[bass.ds(e * CAP, CAP), :]).then_inc(x_loaded[par], 16)

            def store_y(e, par):
                sp.wait_ge(y_sb, e + 2)
                sp.dma_start(ybuf[bass.ds(e * CAP, CAP), :], m.y[par][:]).then_inc(y_stored[par], 16)

            for par in range(2):
                load_gate_up(par, par)
                load_down(par, par)
            sp.wait_ge(scattered, 16 * NT * TOPK)
            load_x(0, 0)
            load_x(1, 1)
            sp.wait_ge(xeT_mm, 1)
            load_x(2, 0)

            def refill_first(e, par, tokens=True):
                sp.wait_ge(gu_mm, e + 1)
                if tokens:
                    load_x(e + 3, 1 - par)
                load_gate_up(e + 2, par)

            def refill_second(e, par, weights=True):
                if weights:
                    sp.wait_ge(y_mm, e + 1)
                    load_down(e + 2, par)
                store_y(e, par)

            refill_first(0, 0)
            with sp.Fori(0, EP - 2) as i:
                for par in (1, 0):
                    e = i * 2 + (2 - par)
                    refill_first(e, par)
                    refill_second(e + (-1), 1 - par)
            refill_first(E - 3, 1, tokens=False)
            for e in range(E - 4, E):
                refill_second(e, e % 2, weights=e < E - 2)
            rows = out.rearrange("(i p) d -> i p d", p=P)
            for i in range(NT):
                sp.wait_ge(acc_done, i + 1)
                sp.dma_start(rows[i], m.acc[:, i, :]).then_inc(stored, 16)
            sp.wait_ge(stored, 16 * NT)

        @block.gpsimd
        def _(pool):
            g = nc.gpsimd
            g.iota(m.lanes_i[:], [[1, E]], base=0, channel_multiplier=0).then_inc(consts, 1)
            g.iota(m.flat_i[:], [[P * TOPK, NT], [1, TOPK]], base=TRASH, channel_multiplier=TOPK).then_inc(consts, 1)
            g.memset(m.ones[:], 1.0).then_inc(consts, 1)
            pool.wait_ge(consts, 3)
            g.affine_select(out=m.before[:], in_=m.ones[:], compare_op=ALU.is_gt, fill=0.0, base=0,
                            pattern=[[1, P]], channel_multiplier=-1).then_inc(consts, 1)
            pool.wait_ge(m.x_zeroed, 16 * 4)
            pool.wait_ge(dest_ready, 1)
            pool.wait_ge(xn_ready, NT)
            for i in range(NT):
                for k in range(TOPK):
                    j = i * TOPK + k
                    g.indirect_dma_start(out=xbuf[:, :], out_offset=bass.IndirectOffsetOnAxis(ap=m.dest[:, j:j + 1], axis=0),
                                         in_=m.xn[:, i, :], in_offset=None).then_inc(scattered, 16)
            for par in range(2):
                pool.wait_ge(y_stored[par], 16 * (EP + 1))
            for i in range(NT):
                if i >= 2:
                    pool.wait_ge(acc_done, i - 1)
                for k in range(TOPK):
                    j = i * TOPK + k
                    g.indirect_dma_start(out=m.got[i % 2][:, k, :], out_offset=None, in_=ybuf[:, :],
                                         in_offset=bass.IndirectOffsetOnAxis(ap=m.frm[:, j:j + 1], axis=0)
                                         ).then_inc(gathered[i % 2], 16)

        @block.tensor
        def _(pe):
            mm, tr = nc.tensor.matmul, nc.tensor.transpose
            for i in range(NT):
                if i >= 2:
                    pe.wait_ge(ss_done, i - 1)
                for h in range(DH):
                    last = tr(m.ps[i % 2][:, h * P:h * P + P], hT[:, h, i * P:i * P + P], m.ident[:])
                last.then_inc(hT_mm, 1)
            for i in range(NT):
                pe.wait_ge(xn_ready, i + 1)
                if i >= 2:
                    pe.wait_ge(xnT_sb, i - 1)
                for h in range(DH):
                    last = tr(m.ps[2 + i % 2][:, h * P:h * P + P], m.xn[:, i, h * P:h * P + P], m.ident[:])
                last.then_inc(xnT_mm, 1)
            pe.wait_ge(xnT_sb, NT)
            pe.wait_ge(loaded, 16 * (len(LOADS) + len(FC)))
            for i in range(NT):
                for k in range(DH):
                    last = mm(m.ps[4][:, i * (E + 1):(i + 1) * (E + 1)], m.xnT[:, k, i * P:i * P + P], m.wr[:, k, :],
                              start=(k == 0), stop=(k == DH - 1))
            last.then_inc(rt_mm, 1)

            def shared(j):
                c, half = STEPS[j]
                n, cols = FC[c], slice(half * 512, half * 512 + 512)
                if j >= 2:
                    pe.wait_ge(sh_h, j - 1)
                for o, w in ((0, m.swg), (1, m.swu)):
                    for k in range(DH):
                        last = mm(m.ps[2 * (j % 2) + o][0:n, 0:512], w[:, k, c * P:c * P + n], m.xnT[:, k, cols],
                                  start=(k == 0), stop=(k == DH - 1))
                last.then_inc(sh_mm, 1)

            shared(0)
            shared(1)
            pe.wait_ge(picked_ready, 1)
            pe.wait_ge(consts, 4)
            picks = m.picked[:].rearrange("p i e -> p (i e)")
            mm(m.ps[5][:, 0:NT * E], m.before[:], picks, start=True, stop=False, skip_group_check=True)
            for d in range(1, NT):
                last = mm(m.ps[5][:, d * E:NT * E], m.ones[:], picks[:, 0:(NT - d) * E], start=False, stop=(d == NT - 1),
                          skip_group_check=True)
            last.then_inc(pos_mm, 1)
            for j in range(2, len(STEPS)):
                shared(j)
            pe.wait_ge(res_ready, 1)
            for i in range(NT):
                if i >= 2:
                    pe.wait_ge(res_sb, i - 1)
                for h in range(DH):
                    last = tr(m.ps[4 + i % 2][:, h * P:h * P + P], m.resT[:, h, i * P:i * P + P], m.ident[:])
                last.then_inc(res_mm, 1)
            pe.wait_ge(sh_h, len(STEPS))
            for i in range(NT):
                if i >= 2:
                    pe.wait_ge(acc_ready, i - 1)
                for c, n in enumerate(FC):
                    last = mm(m.ps[6 + i % 2][:, 0:D], m.shT[0:n, c, i * P:i * P + P], m.swd[0:n, c, :],
                              start=(c == 0), stop=(c == len(FC) - 1))
                last.then_inc(shd_mm, 1)

            pe.wait_ge(acc_ready, NT)
            pe.wait_ge(res_sb, NT)

            def transpose_x(e, par, loads):
                pe.wait_ge(x_loaded[par], loads)
                for h in range(DH):
                    last = tr(m.ps[0][:, h * P:h * P + P], m.xe[par][:, h * P:h * P + P], m.ident[:])
                last.then_inc(xeT_mm, 1)

            def gate_up(e, par, loads):
                pe.wait_ge(gu_loaded[par], loads)
                pe.wait_ge(xeT_sb, e + 1)
                for k in range(DH):
                    last = mm(m.ps[1][:, 0:2 * F], m.xeT[par][:, k, :], m.wgu[par][:, k, :], start=(k == 0), stop=(k == DH - 1))
                last.then_inc(gu_mm, 1)

            def transpose_h(e):
                pe.wait_ge(eh_sb, e + 1)
                for c in range(2):
                    last = tr(m.ps[2][0:FH, c * P:c * P + P], m.eh[:, c * FH:c * FH + FH], m.ident[:])
                last.then_inc(ehT_mm, 1)

            def down(e, par, loads):
                pe.wait_ge(dn_loaded[par], loads)
                pe.wait_ge(ehT_sb, e + 1)
                pe.wait_ge(y_sb, e + 1)
                for c in range(2):
                    last = mm(m.ps[3][:, 0:D], m.ehT[0:FH, c, :], m.wdn[par][0:FH, c, :], start=(c == 0), stop=(c == 1))
                last.then_inc(y_mm, 1)

            transpose_x(0, 0, 16)
            pe.wait_ge(xeT_sb, 1)
            transpose_x(1, 1, 16)
            gate_up(0, 0, 16)
            pe.wait_ge(xeT_sb, 2)
            transpose_x(2, 0, 32)

            def expert(e, par, turn, following=True, tokens=True):
                transpose_h(e)
                if following:
                    gate_up(e + 1, 1 - par, turn + 16 * (1 + par))
                down(e, par, turn + 16)
                if tokens:
                    pe.wait_ge(xeT_sb, e + 3)
                    transpose_x(e + 3, 1 - par, turn + 16 * (2 + par))

            with pe.Fori(0, EP - 2) as i:
                for par in range(2):
                    expert(i * 2 + par, par, i * 16)
            for e in range(E - 4, E):
                expert(e, e % 2, e // 2 * 16, following=e < E - 1, tokens=e < E - 3)

        @block.scalar
        def _(act):
            f = nc.scalar.activation
            for i in range(NT):
                act.wait_ge(hT_mm, i + 1)
                f(m.h_tok[:, i, :], m.ps[i % 2][:, 0:D], ACT.Identity).then_inc(h_sb, 1)
                if i:
                    act.wait_ge(ss_done, i)
                f(m.sq[:], m.ps[i % 2][:, 0:D], ACT.Square, accum_out=m.ss[:, i:i + 1]).then_inc(ss_done, 1)
            act.wait_ge(var_ready, 1)
            f(m.root[:], m.var[:], ACT.Sqrt).then_inc(root_ready, 1)
            for i in range(NT):
                act.wait_ge(xnT_mm, i + 1)
                f(m.xnT[:, :, i * P:i * P + P], m.ps[2 + i % 2][:, 0:D].rearrange("p (h t) -> p h t", h=DH), ACT.Identity
                  ).then_inc(xnT_sb, 1)
            act.wait_ge(lsub_ready, 1)
            f(m.probs[:], m.logits[:, :, 0:E], ACT.Exp).then_inc(lexp_ready, 1)
            act.preload_act_table_set("sigmoid_and_others")
            f(m.gate_s[:], m.logits[:, :, E:E + 1].rearrange("p i o -> p (i o)"), ACT.Sigmoid).then_inc(lexp_ready, 1)
            for j, (c, half) in enumerate(STEPS):
                act.wait_ge(sh_mm, j + 1)
                if j >= 2:
                    act.wait_ge(sh_h, j - 1)
                n = FC[c]
                f(m.ssig[j % 2][0:n, :], m.ps[2 * (j % 2)][0:n, 0:512], ACT.Sigmoid).then_inc(sh_sig, 1)
            for i in range(NT):
                act.wait_ge(res_mm, i + 1)
                f(m.acc[:, i, :], m.ps[4 + i % 2][:, 0:D], ACT.Identity).then_inc(res_sb, 1)
            act.sem_inc(y_sb, 1)
            for par in range(2):
                act.sem_inc(y_stored[par], 16)

            def x_transposed(e, par):
                act.wait_ge(xeT_mm, e + 1)
                f(m.xeT[par][:], m.ps[0][:, 0:D].rearrange("p (h t) -> p h t", h=DH), ACT.Identity).then_inc(xeT_sb, 1)

            def gate(e, par):
                act.wait_ge(gu_mm, e + 1)
                f(m.esig[par][:], m.ps[1][:, 0:F], ACT.Sigmoid).then_inc(sig_sb, 1)

            def result(e, par, stores):
                act.wait_ge(y_mm, e + 1)
                act.wait_ge(y_stored[par], stores)
                f(m.y[par][:], m.ps[3][:, 0:D], ACT.Identity).then_inc(y_sb, 1)

            x_transposed(0, 0)
            x_transposed(1, 1)
            gate(0, 0)
            x_transposed(2, 0)

            def expert(e, par, turn, following=True, tokens=True):
                if following:
                    gate(e + 1, 1 - par)
                result(e, par, turn + 16)
                if tokens:
                    x_transposed(e + 3, 1 - par)

            with act.Fori(0, EP - 2) as i:
                for par in range(2):
                    expert(i * 2 + par, par, i * 16)
            for e in range(E - 4, E):
                expert(e, e % 2, e // 2 * 16, following=e < E - 1, tokens=e < E - 3)

        @block.vector
        def _(dve):
            v = nc.vector
            tt, ts, stt = v.tensor_tensor, v.tensor_scalar, v.scalar_tensor_tensor
            n = [0]

            def then(ins):
                ins.then_inc(chain, 1)
                n[0] += 1
                dve.wait_ge(chain, n[0])

            dve.wait_ge(consts, 2)
            then(v.tensor_copy(m.lanes[:], m.lanes_i[:]))
            then(v.tensor_copy(m.flat[:], m.flat_i[:]))
            tt(m.resT[:], x2T, hT, ALU.add).then_inc(res_ready, 1)
            dve.wait_ge(ss_done, NT)
            ts(m.var[:], m.ss[:], 1.0 / D, NORM_EPS, ALU.mult, ALU.add).then_inc(var_ready, 1)
            dve.wait_ge(root_ready, 1)
            then(v.reciprocal(m.rstd[:], m.root[:]))
            then(tt(m.newt[:], m.rstd[:], m.rstd[:], ALU.mult))
            then(tt(m.newt[:], m.newt[:], m.var[:], ALU.mult))
            then(ts(m.newt[:], m.newt[:], -0.5, 1.5, ALU.mult, ALU.add))
            then(tt(m.rstd[:], m.rstd[:], m.newt[:], ALU.mult))
            dve.wait_ge(loaded, 16 * (len(LOADS) + len(FC)))
            dve.wait_ge(h_sb, NT)
            for i in range(NT):
                stt(out=m.xn[:, i, :], in0=m.h_tok[:, i, :], scalar=m.rstd[:, i:i + 1], in1=m.wn[:], op0=ALU.mult,
                    op1=ALU.mult).then_inc(xn_ready, 1)
            dve.wait_ge(rt_mm, 1)
            then(v.tensor_copy(m.logits[:], m.ps[4][:, 0:NT * (E + 1)].rearrange("p (i e) -> p i e", i=NT)))
            then(v.tensor_reduce(m.lmax[:], m.logits[:, :, 0:E], AX.X, ALU.max))
            wide = lambda x: x.unsqueeze(2).broadcast_to((P, NT, E))
            tt(m.logits[:, :, 0:E], m.logits[:, :, 0:E], wide(m.lmax[:]), ALU.subtract).then_inc(lsub_ready, 1)
            dve.wait_ge(lexp_ready, 1)
            then(v.tensor_reduce(m.lsum[:], m.probs[:], AX.X, ALU.add))
            then(v.reciprocal(m.linv[:], m.lsum[:]))
            then(tt(m.probs[:], m.probs[:], wide(m.linv[:]), ALU.mult))
            for i in range(NT):
                then(v.max(m.top8[:, i, :], m.probs[:, i, :]))
                then(v.max_index(m.idx8[:, i, :], m.top8[:, i, :], m.probs[:, i, :]))
            then(v.tensor_copy(m.idxf[:], m.idx8[:, :, 0:TOPK]))
            for k in range(TOPK):
                then(tt(m.hot[:, :, k, :], m.lanes[:].unsqueeze(1).broadcast_to((P, NT, E)),
                        m.idxf[:, :, k:k + 1].broadcast_to((P, NT, E)), ALU.is_equal))
            then(v.tensor_reduce(m.picked_f[:], m.hot[:].rearrange("p i k e -> p i e k"), AX.X, ALU.add))
            v.tensor_copy(m.picked[:], m.picked_f[:]).then_inc(picked_ready, 1)
            dve.wait_ge(pos_mm, 1)
            pos = m.ps[5][:, 0:NT * E].rearrange("p (i e) -> p i e", i=NT)
            for k in range(TOPK):
                then(tt(m.hotpos[:, :, k, :], m.hot[:, :, k, :], pos, ALU.mult))
            then(v.tensor_reduce(m.posk[:], m.hotpos[:], AX.X, ALU.add))
            then(ts(m.valid[:], m.posk[:], float(CAP), None, ALU.is_lt))
            then(tt(m.wk[:], m.top8[:, :, 0:TOPK], m.valid[:], ALU.mult))
            then(stt(out=m.slot[:], in0=m.idxf[:], scalar=float(CAP), in1=m.posk[:], op0=ALU.mult, op1=ALU.add))
            then(tt(m.dest_f[:], m.slot[:], m.flat[:], ALU.subtract))
            then(tt(m.dest_f[:], m.dest_f[:], m.valid[:], ALU.mult))
            then(tt(m.dest_f[:], m.dest_f[:], m.flat[:], ALU.add))
            then(ts(m.posk[:], m.posk[:], float(CAP - 1), None, ALU.min))
            then(stt(out=m.from_f[:], in0=m.idxf[:], scalar=float(CAP), in1=m.posk[:], op0=ALU.mult, op1=ALU.add))
            then(v.tensor_copy(m.frm[:], m.from_f[:].rearrange("p i k -> p (i k)")))
            v.tensor_copy(m.dest[:], m.dest_f[:].rearrange("p i k -> p (i k)")).then_inc(dest_ready, 1)
            for j, (c, half) in enumerate(STEPS):
                k = FC[c]
                dve.wait_ge(sh_sig, j + 1)
                if j:
                    dve.wait_ge(sh_h, j)
                then(tt(m.sgate[0:k, :], m.ssig[j % 2][0:k, :], m.ps[2 * (j % 2)][0:k, 0:512], ALU.mult))
                tt(m.shT[0:k, c, half * 512:half * 512 + 512], m.sgate[0:k, :], m.ps[2 * (j % 2) + 1][0:k, 0:512],
                   ALU.mult).then_inc(sh_h, 1)
            dve.wait_ge(lexp_ready, 2)
            for i in range(NT):
                dve.wait_ge(shd_mm, i + 1)
                dve.wait_ge(res_sb, i + 1)
                stt(out=m.acc[:, i, :], in0=m.ps[6 + i % 2][:, 0:D], scalar=m.gate_s[:, i:i + 1], in1=m.acc[:, i, :],
                    op0=ALU.mult, op1=ALU.add).then_inc(acc_ready, 1)
            def hidden(e, par):
                dve.wait_ge(sig_sb, e + 1)
                tt(m.eg[:], m.esig[par][:], m.ps[1][:, 0:F], ALU.mult).then_inc(echain, 1)
                dve.wait_ge(echain, e + 1)
                tt(m.eh[:], m.eg[:], m.ps[1][:, F:2 * F], ALU.mult).then_inc(eh_sb, 1)

            def hidden_transposed(e):
                dve.wait_ge(ehT_mm, e + 1)
                v.tensor_copy(m.ehT[:], m.ps[2][0:FH, 0:2 * P].rearrange("p (c t) -> p c t", c=2)).then_inc(ehT_sb, 1)

            hidden(0, 0)
            with dve.Fori(0, EP - 1) as i:
                for par in range(2):
                    e = i * 2 + par
                    hidden_transposed(e)
                    hidden(e + 1, 1 - par)
            hidden_transposed(E - 2)
            hidden(E - 1, 1)
            hidden_transposed(E - 1)
            dve.wait_ge(acc_ready, NT)
            for i in range(NT):
                dve.wait_ge(gathered[i % 2], 16 * TOPK * (i // 2 + 1))
                for k in range(TOPK):
                    ins = stt(out=m.acc[:, i, :], in0=m.got[i % 2][:, k, :], scalar=m.wk[:, i, k:k + 1], in1=m.acc[:, i, :],
                              op0=ALU.mult, op1=ALU.add)
                    if k == TOPK - 1:
                        ins.then_inc(acc_done, 1)
                    else:
                        then(ins)


def _layouts(i):
    f = lambda n: np.asarray(i[n])
    rows = lambda w: w.reshape(w.shape[0] // P, P, w.shape[1]).transpose(1, 0, 2)
    cols = lambda b: b.reshape(-1, P).T
    x = f("x")
    a = {
        "x": x.transpose(2, 1, 0).reshape(DH, P, T, B).transpose(1, 2, 0, 3).reshape(P, T, S8),
        "cond": f("cond_2048").T.reshape(DH, P, B).transpose(1, 0, 2).reshape(P, S8),
        "couple": rows(f("L0_cond_coupling").T),
        "bias": cols(f("L0_cond_bias")),
        "whh": rows(f("L0_cond2_W_hh")), "wih": rows(f("L0_cond2_W_ih")),
        "bhh": cols(f("L0_cond2_b_hh")), "bih": cols(f("L0_cond2_b_ih")),
    }
    heads = lambda w: rows(w).reshape(P, DH, NH, HD).transpose(2, 0, 1, 3).reshape(NH, P, DH * HD)
    head_cols = lambda b: b.reshape(NH, HD, 1)
    w = "L0_attn_w_"
    a["wqkv"] = np.concatenate([heads(f(w + c)) for c in "qkv"] + [head_cols(f(f"L0_attn_b_{c}")) for c in "qkv"], axis=2)
    ffn = lambda n: f("L0_ffn_" + n)
    experts = lambda n: ffn(n).reshape(E, DH, P, F).transpose(0, 2, 1, 3)
    a["wgu"] = np.concatenate([experts("w_gate"), experts("w_up")], axis=3).reshape(E, P, DH * 2 * F)
    a["wdn"] = ffn("w_down").reshape(E, 2, F // 2, D).transpose(0, 2, 1, 3).reshape(E, F // 2, 2 * D)
    a["wr"] = np.concatenate([rows(ffn("w_router")), rows(ffn("w_shared_gate"))], axis=2)
    a["wn"] = np.broadcast_to(ffn("w_norm"), (P, D))
    a["swg"], a["swu"], a["swd"] = rows(ffn("sw_gate")), rows(ffn("sw_up")), ffn("sw_down")
    a["wo"] = rows(f("L0_attn_w_o"))
    a["bo"] = cols(f("L0_attn_b_o"))
    return {k: np.ascontiguousarray(v) for k, v in a.items()}


def program(nc, a, out):
    kv = nc.dram_tensor("kv_scratch", (NH, P, 2 * B * TB), F32, kind="Internal").ap()
    xbuf = nc.dram_tensor("x_exchange", (E * CAP + N * TOPK, D), F32, kind="Internal").ap()
    ybuf = nc.dram_tensor("y_exchange", (E * CAP, D), F32, kind="Internal").ap()
    with ExitStack() as ctx:
        m = Memory(nc, ctx)
        allocate_scans(m)
        with ExitStack() as m.ctx:
            allocate_attention(m)
            setup(nc, m, a, xbuf)
            scan_block(nc, m, "s0", 0, None)
            attention_block(nc, m, a, kv, 0)
            scan_block(nc, m, "s1", TB, 0)
            attention_block(nc, m, a, kv, 1)
            gru_block(nc, m, "s2", TB)
        m.ctx = ctx
        allocate_moe(m)
        moe(nc, m, a, xbuf, ybuf, out)


def kernel(**inputs):
    import concourse.bacc as bacc
    from concourse.bass_utils import run_bass_kernel_spmd

    nc = bacc.Bacc("TRN2", target_bir_lowering=False, num_devices=1)
    arrays = {"in_" + k: v for k, v in _layouts(inputs).items()}
    a = {k[3:]: nc.dram_tensor(k, v.shape, mybir.dt.from_np(v.dtype), kind="ExternalInput").ap() for k, v in arrays.items()}
    out = nc.dram_tensor("out", (N, D), F32, kind="ExternalOutput").ap()
    program(nc, a, out)
    result = run_bass_kernel_spmd(nc, [arrays], core_ids=[0])
    return result.results[0]["out"].reshape(B, T, D)
```
